# Optimizing a Trainium2 kernel written in Bass

```python
import numpy as np
import jax
import jax.numpy as jnp

def _softmax(x, axis=-1):
    return jax.nn.softmax(x, axis=axis)

def _gelu(x):
    return jax.nn.gelu(x, approximate=True)

def _silu(x):
    return jax.nn.silu(x)

def _sigmoid(x):
    return jax.nn.sigmoid(x)

def _layernorm(x, axis=-1, eps=1e-05):
    m = jnp.mean(x, axis=axis, keepdims=True)
    v = jnp.var(x, axis=axis, keepdims=True)
    return (x - m) / jnp.sqrt(v + eps)

def _scatter_add(tgt, idx, src, axis=0):
    return tgt.at[idx].add(src)

def _segment_sum(src, seg, n):
    return jax.ops.segment_sum(src, seg, n)
kernel_name = 'mk_rec_standalone_d1_rec_r8_cd14e1'

def setup_inputs(seed: int=0):
    np.random.seed(seed)
    _w = jnp.asarray

    def _rec_inputs():
        import jax
        import jax.numpy as jnp
        _rk = jax.random.key(seed)
        r_F = -7.10856e-05 + 0.999911 * jax.random.normal(jax.random.fold_in(_rk, 1), (2048, 64, 128), jnp.float32)
        return r_F
    r_F = _rec_inputs()

    def _L0_rec_setup():
        import jax, jax.numpy as jnp
        import numpy as np
        B, NF, D = (1024, 64, 128)
        key = jax.random.key(seed)
        k1, k2, k3, k4 = jax.random.split(key, 4)
        F = jax.random.normal(k1, (B, NF, D), dtype=jnp.float32)
        W = jax.random.normal(k2, (NF, NF, D), dtype=jnp.float32) * 0.05
        K_w = jax.random.normal(k3, (D, D), dtype=jnp.float32) * (1.0 / np.sqrt(D))
        Q_w = jax.random.normal(k4, (D, D), dtype=jnp.float32) * (1.0 / np.sqrt(D))
        return {'F': F, 'W': W, 'K_w': K_w, 'Q_w': Q_w}
    _L0_rec_all = _L0_rec_setup()
    _L0_rec_in = {k: v for k, v in _L0_rec_all.items() if k in ('W', 'K_w', 'Q_w')}
    del _L0_rec_all
    return {'r_F': r_F, 'L0_rec_W': _L0_rec_in['W'], 'L0_rec_K_w': _L0_rec_in['K_w'], 'L0_rec_Q_w': _L0_rec_in['Q_w']}

def reference(r_F, L0_rec_W, L0_rec_K_w, L0_rec_Q_w):
    import jax
    import jax.numpy as jnp

    def _L0_rec_ref(F, W, K_w, Q_w):
        import jax, jax.numpy as jnp
        import numpy as np
        B, NF, D = (1024, 64, 128)
        Kf = jnp.einsum('bjd,ed->bje', F, K_w)
        S = jnp.einsum('bid,bjd->bij', F, Kf)
        out = jnp.einsum('bij,ijd->bid', S, W)
        out = out + jnp.einsum('bid,ed->bie', F, Q_w)
        return out
    y = _L0_rec_ref(r_F, L0_rec_W, L0_rec_K_w, L0_rec_Q_w)
    return y

_drawn_inputs = setup_inputs


def setup_inputs(seed=0):
    import zlib

    import numpy as np

    out = dict(_drawn_inputs(seed))
    spreads = {}
    factors = {}
    for name, (base, spread) in spreads.items():
        noise = np.random.default_rng([zlib.crc32(name.encode()), seed]).standard_normal(out[name].shape)
        drawn = base * np.exp(spread * noise) if base else spread * noise
        out[name] = jnp.asarray(drawn.astype(out[name].dtype))
    for name, factor in factors.items():
        out[name] = (out[name] * factor).astype(out[name].dtype)
    return out
```

```python
from contextlib import ExitStack

import concourse.bass as bass
from concourse import mybir

F32 = mybir.dt.float32
F32R = mybir.dt.float32r
ALU = mybir.AluOpType
COPY = mybir.ActivationFunctionType.Copy

P = 128
D = 128
N = 64
B = 2048
TILES = B // P
CB = 8
CHUNK = CB * N
STEPS = P // CB
IR = N // STEPS
FRONT = TILES * STEPS
PAIR = 2 * N
GROUP = 8
GROUPS = FRONT // GROUP
LAG = STEPS // GROUP
LOADS = 4
OBUF = 2
WPIECES = 8
WROWS = N // WPIECES


def build(nc, f_t, k_t, q_t, w, out):
    with ExitStack() as ctx:
        def sbuf(name, shape, dt=F32):
            return ctx.enter_context(nc.sbuf_tensor(name, shape, dt))

        def psum(name, shape):
            return ctx.enter_context(nc.psum_tensor(name, shape, F32))

        def sem(name):
            return ctx.enter_context(nc.semaphore(name))

        f_ring = sbuf("f_ring", [D, LOADS * 2, CHUNK])
        f_hi = sbuf("f_hi", [D, CHUNK], F32R)
        f_lo = sbuf("f_lo", [D, CHUNK], F32R)
        kf = sbuf("kf", [D, 2, CHUNK])
        s_t = sbuf("s_t", [P, N, 2 * P], F32R)
        f_q = sbuf("f_q", [D, N, 2 * P])
        w_hl = sbuf("w_hl", [P, N, 2 * D], F32R)
        k_raw = sbuf("k_raw", [D, D])
        k_hi = sbuf("k_hi", [D, D], F32R)
        k_lo = sbuf("k_lo", [D, D], F32R)
        q_sb = sbuf("q_sb", [D, D])
        o_sb = sbuf("o_sb", [P, OBUF, IR * D])
        w_raw = f_q[:, :, P:2 * P]

        kf_ps = psum("kf_ps", [D, 2, CHUNK])
        s_ps = psum("s_ps", [P, 2, CB // 2, PAIR])
        o_ps = psum("o_ps", [P, 2, IR, 2 * D])

        f_in = [sem(f"f_in{n}") for n in range(LOADS)]
        k_in, q_in = sem("k_in"), sem("q_in")
        w_in = [sem(f"w_in{n}") for n in range(WPIECES)]
        o_stored = [sem(f"o_stored{n}") for n in range(OBUF)]
        k_split = sem("k_split")
        fhi_done = sem("fhi_done")
        flo_done = sem("flo_done")
        kf_done = sem("kf_done")
        kf_copied = sem("kf_copied")
        s_done = sem("s_done")
        shi_done = sem("shi_done")
        slo_done = sem("slo_done")
        fq_done = sem("fq_done")
        whi_done = sem("whi_done")
        wlo_done = sem("wlo_done")
        o_done = sem("o_done")
        ohi_done = sem("ohi_done")
        out_done = sem("out_done")

        def arrived(eng, g, r):
            turn = (g - r) // GROUP if isinstance(g, int) else (g - r) >> 3
            eng.wait_ge(f_in[r // 2], turn * 16 + 16)

        def wait(eng, semaphore, count):
            if not (isinstance(count, int) and count <= 0):
                eng.wait_ge(semaphore, count)

        def groups(eng, step):
            def one(j):
                base = j * GROUP
                col = (j % 4) * (GROUP * CB) if isinstance(j, int) else (j & 3) * (GROUP * CB)
                static = isinstance(j, int)
                for r in range(GROUP):
                    step(j, base, r, col, not static or j < GROUPS, not static or j >= LAG)
            for j in range(LAG + 1):
                one(j)
            with eng.Fori(LAG + 1, GROUPS - 1) as j:
                one(j)
            for j in range(GROUPS - 1, GROUPS + LAG):
                one(j)

        block = ctx.enter_context(nc.Block())

        @block.sync
        def _(sp):
            w_jid = w.rearrange("i j d -> j i d")

            def load_f(m, slot):
                sp.dma_start(f_ring[:, 2 * slot:2 * slot + 2, :],
                             f_t[bass.ds(m, 1), :, :, :].rearrange("o d c n -> (o d) c n")
                             ).then_inc(f_in[slot], 16)

            def load_w(n):
                rows = slice(n * WROWS, (n + 1) * WROWS)
                for half in range(2):
                    sp.dma_start(w_raw[half * N:(half + 1) * N, rows, :], w_jid[:, rows, :]
                                 ).then_inc(w_in[n], 16)

            def store(tile, i0, r, h):
                sp.wait_ge(out_done, h + 3)
                dst = out[bass.ds(tile * P, P), bass.ds(i0, IR), :]
                sp.dma_start(dst, o_sb[:, r % OBUF, :].rearrange("p (i d) -> p i d", i=IR)
                             ).then_inc(o_stored[r % OBUF], 16)

            load_f(0, 0)
            sp.dma_start(k_raw[:, :], k_t).then_inc(k_in, 16)
            for m in range(1, LOADS - 1):
                load_f(m, m)
            sp.dma_start(q_sb[:, :], q_t).then_inc(q_in, 16)

            def step(j, base, r, col, front, back):
                static = isinstance(j, int)
                if r % 2 == 0 and not (static and base + r + 6 >= FRONT):
                    wait(sp, s_done, base + r)
                    wait(sp, fq_done, base + r)
                    load_f(j * 4 + (r + 6) // 2, (r // 2 + 3) % LOADS)
                if static and j < LAG and 8 * j + r < WPIECES:
                    load_w(8 * j + r)
                if static:
                    h = base + r - STEPS - 1
                    if h >= 0:
                        store(h // STEPS, (h % STEPS) * IR, h % GROUP, h)
                elif r == 0:
                    store((j - LAG - 1) >> 1, ((j - LAG - 1) & 1) * (GROUP * IR) + (GROUP - 1) * IR,
                          GROUP - 1, base - STEPS - 1)
                else:
                    store((j - LAG) >> 1, ((j - LAG) & 1) * (GROUP * IR) + (r - 1) * IR,
                          r - 1, base + (r - 1 - STEPS))

            groups(sp, step)
            store(TILES - 1, (STEPS - 1) * IR, GROUP - 1, FRONT - 1)
            for n in range(OBUF):
                sp.wait_ge(o_stored[n], 16 * (FRONT // OBUF))

        @block.scalar
        def _(act):
            def split_f(g, r):
                arrived(act, g, r)
                wait(act, kf_done, g)
                nc.scalar.activation(f_hi[:, :], f_ring[:, r, :], COPY).then_inc(fhi_done, 1)

            def copy_kf(g, r):
                act.wait_ge(kf_done, g + 1)
                wait(act, s_done, g - 1)
                nc.scalar.activation(kf[:, r % 2, :], kf_ps[:, r % 2, :], COPY).then_inc(kf_copied, 1)

            def store_s_hi(g, r, col):
                act.wait_ge(s_done, g + 1)
                for half in range(2):
                    rows = slice(half * N, (half + 1) * N)
                    ins = nc.scalar.activation(
                        s_t[rows, :, bass.ds(col + (r * CB + 4 * half), 4)],
                        s_ps[rows, r % 2, :, rows].rearrange("p k i -> p i k"), COPY)
                ins.then_inc(shi_done, 1)

            def copy_out_hi(h, r):
                act.wait_ge(o_done, h + 1)
                wait(act, o_stored[r % OBUF], (h - r % OBUF) * (16 // OBUF))
                nc.scalar.activation(o_sb[:, r % OBUF, :].rearrange("p (i d) -> p i d", i=IR),
                                     o_ps[:, r % 2, :, 0:D], COPY).then_inc(ohi_done, 1)

            act.wait_ge(k_in, 16)
            nc.scalar.activation(k_hi[:, :], k_raw[:, :], COPY).then_inc(k_split, 1)
            split_f(0, 0)
            split_f(1, 1)
            copy_kf(0, 0)

            def step(j, base, r, col, front, back):
                static = isinstance(j, int)
                g = base + r
                if back and not (static and g == STEPS):
                    copy_out_hi(base + (r - STEPS - 1), (r - 1) % GROUP)
                if front and not (static and g + 1 >= FRONT):
                    copy_kf(base + (r + 1), (r + 1) % GROUP)
                if front and not (static and g + 2 >= FRONT):
                    split_f(base + (r + 2), (r + 2) % GROUP)
                if static and 1 <= g <= WPIECES:
                    n = g - 1
                    rows = slice(n * WROWS, (n + 1) * WROWS)
                    act.wait_ge(w_in[n], 32)
                    nc.scalar.activation(w_hl[:, rows, 0:D], w_raw[:, rows, :], COPY).then_inc(whi_done, 1)
                if front:
                    if r == 0:
                        wait(act, o_done, base - STEPS)
                    store_s_hi(g, r, col)

            groups(act, step)
            copy_out_hi(FRONT - 1, GROUP - 1)

        @block.vector
        def _(dve):
            def split_f(g, r):
                dve.wait_ge(fhi_done, g + 1)
                wait(dve, kf_done, g)
                nc.vector.tensor_tensor(f_lo[:, :], f_ring[:, r, :], f_hi[:, :].bitcast(F32),
                                        ALU.subtract).then_inc(flo_done, 1)

            def store_s_lo(g, r, col):
                dve.wait_ge(shi_done, g + 1)
                for half in range(2):
                    rows = slice(half * N, (half + 1) * N)
                    other = slice((1 - half) * N, (2 - half) * N)
                    cols = bass.ds(col + (r * CB + 4 * half), 4)
                    ins = nc.vector.tensor_tensor(
                        s_t[other, :, cols],
                        s_ps[rows, r % 2, :, rows].rearrange("p k i -> p i k"),
                        s_t[rows, :, cols].bitcast(F32), ALU.subtract)
                ins.then_inc(slo_done, 1)

            def sum_out(h, r):
                dve.wait_ge(ohi_done, h + 1)
                o_view = o_sb[:, r % OBUF, :].rearrange("p (i d) -> p i d", i=IR)
                nc.vector.tensor_tensor(o_view, o_ps[:, r % 2, :, D:2 * D], o_view,
                                        ALU.add).then_inc(out_done, 1)

            dve.sem_inc(out_done, 2)
            dve.wait_ge(k_split, 1)
            nc.vector.tensor_tensor(k_lo[:, :], k_raw[:, :], k_hi[:, :].bitcast(F32),
                                    ALU.subtract).then_inc(k_split, 1)
            split_f(0, 0)
            split_f(1, 1)

            def step(j, base, r, col, front, back):
                static = isinstance(j, int)
                g = base + r
                if back and not (static and g == STEPS):
                    sum_out(base + (r - STEPS - 1), (r - 1) % GROUP)
                if front and not (static and g + 2 >= FRONT):
                    split_f(base + (r + 2), (r + 2) % GROUP)
                if front:
                    store_s_lo(g, r, col)

            groups(dve, step)
            sum_out(FRONT - 1, GROUP - 1)

        @block.gpsimd
        def _(pool):
            def copy_fq(g, r, col):
                arrived(pool, g, r)
                nc.gpsimd.tensor_copy(
                    f_q[:, :, bass.ds(col + r * CB, CB)].rearrange("d i (h k) -> d i h k", h=2),
                    f_ring[:, r, :].rearrange("d (k h i) -> d i h k", k=4, h=2)).then_inc(fq_done, 1)

            def step(j, base, r, col, front, back):
                static = isinstance(j, int)
                g = base + r
                if static and 2 <= g <= WPIECES + 1:
                    n = g - 2
                    rows = slice(n * WROWS, (n + 1) * WROWS)
                    pool.wait_ge(whi_done, n + 1)
                    nc.gpsimd.tensor_tensor(w_hl[:, rows, D:2 * D], w_raw[:, rows, :],
                                            w_hl[:, rows, 0:D].bitcast(F32),
                                            ALU.subtract).then_inc(wlo_done, 1)
                if front:
                    if static and g == STEPS:
                        pool.wait_ge(wlo_done, WPIECES)
                    if r == 0:
                        wait(pool, o_done, base - STEPS)
                    copy_fq(g, r, col)

            groups(pool, step)

        @block.tensor
        def _(pe):
            def project(g, n):
                pe.wait_ge(flo_done, g + 1)
                wait(pe, kf_copied, g - 1)
                dst = kf_ps[:, n % 2, :]
                nc.tensor.matmul(dst, k_hi[:, :], f_hi[:, :], start=True, stop=False)
                nc.tensor.matmul(dst, k_hi[:, :], f_lo[:, :], start=False, stop=False)
                nc.tensor.matmul(dst, k_lo[:, :], f_hi[:, :], start=False, stop=True
                                 ).then_inc(kf_done, 1)

            def scores(g, n):
                pe.wait_ge(kf_copied, g + 1)
                wait(pe, slo_done, g - 1)
                for k in range(CB // 2):
                    cols = slice(k * PAIR, (k + 1) * PAIR)
                    ins = nc.tensor.matmul(s_ps[:, n % 2, k, :], kf[:, n % 2, cols],
                                           f_ring[:, n % GROUP, cols], start=True, stop=True)
                ins.then_inc(s_done, 1)

            def rows_out(tile_parity, n, half):
                for x in range(2 * half, 2 * half + 2):
                    i = n * IR + x
                    cols = slice(tile_parity * P, (tile_parity + 1) * P)
                    nc.tensor.matmul(o_ps[:, n % 2, x, :], s_t[:, i, cols], w_hl[:, i, :],
                                     start=True, stop=False, skip_group_check=True)
                    ins = nc.tensor.matmul(o_ps[:, n % 2, x, 0:D], f_q[:, i, cols], q_sb[:, :],
                                           start=False, stop=True, skip_group_check=True)
                if half == 1:
                    ins.then_inc(o_done, 1)

            def tile(base, parity, front=True, back=True, last=False):
                for n in range(STEPS):
                    g = base + n
                    if front and not (last and n == STEPS - 1):
                        project(base + (n + 1), n + 1)
                    if back:
                        if n == 0:
                            pe.wait_ge(slo_done, base)
                            pe.wait_ge(fq_done, base)
                        pe.wait_ge(out_done, base + (n - STEPS + 1))
                        rows_out(1 - parity, n, 0)
                    if front:
                        scores(g, n)
                    if back:
                        rows_out(1 - parity, n, 1)

            pe.wait_ge(k_split, 2)
            project(0, 0)
            tile(0, 0, back=False)
            pe.wait_ge(q_in, 16)
            pe.wait_ge(whi_done, WPIECES)
            pe.wait_ge(wlo_done, WPIECES)
            with pe.Fori(0, TILES // 2 - 1) as pair:
                base = pair * (2 * STEPS) + STEPS
                tile(base, 1)
                tile(base + STEPS, 0)
            tile(FRONT - STEPS, 1, last=True)
            tile(FRONT, 0, front=False)


def kernel(r_F, L0_rec_W, L0_rec_K_w, L0_rec_Q_w):
    import numpy as np
    import concourse.bacc as bacc
    from concourse.bass_utils import run_bass_kernel_spmd

    f = np.asarray(r_F).reshape(FRONT // 2, 2, 2, CB // 2, N, D)
    f_t = np.ascontiguousarray(f.transpose(0, 5, 1, 3, 2, 4)).reshape(FRONT // 2, D, 2, CHUNK)
    arrays = {
        "f_t": f_t,
        "k_t": np.ascontiguousarray(np.asarray(L0_rec_K_w).T),
        "q_t": np.ascontiguousarray(np.asarray(L0_rec_Q_w).T),
        "w": np.ascontiguousarray(np.asarray(L0_rec_W)),
    }
    nc = bacc.Bacc("TRN2", target_bir_lowering=False, num_devices=1, dynamic_dma_scratch_size=1024)
    args = [nc.dram_tensor(n, a.shape, F32, kind="ExternalInput").ap() for n, a in arrays.items()]
    out = nc.dram_tensor("out", (B, N, D), F32, kind="ExternalOutput").ap()
    build(nc, *args, out)
    r = run_bass_kernel_spmd(nc, [arrays], core_ids=[0])
    return r.results[0]["out"]
```

```python
from contextlib import ExitStack

import concourse.bass as bass
from concourse import mybir

F32 = mybir.dt.float32
F32R = mybir.dt.float32r
ALU = mybir.AluOpType
COPY = mybir.ActivationFunctionType.Copy

P = 128
D = 128
N = 64
B = 2048
TILES = B // P
CB = 8
CHUNK = CB * N
STEPS = P // CB
IR = N // STEPS
FRONT = TILES * STEPS
PAIR = 2 * N
GROUP = 8
GROUPS = FRONT // GROUP
LAG = STEPS // GROUP
LOADS = 4
OBUF = 2
WPIECES = STEPS
WROWS = N // WPIECES


def build(nc, f_t, k_t, q_t, w, out):
    with ExitStack() as ctx:
        def sbuf(name, shape, dt=F32):
            return ctx.enter_context(nc.sbuf_tensor(name, shape, dt))

        def psum(name, shape):
            return ctx.enter_context(nc.psum_tensor(name, shape, F32))

        def sem(name):
            return ctx.enter_context(nc.semaphore(name))

        f_ring = sbuf("f_ring", [D, LOADS * 2, CHUNK])
        f_hi = sbuf("f_hi", [D, CHUNK], F32R)
        f_lo = sbuf("f_lo", [D, CHUNK], F32R)
        kf = sbuf("kf", [D, 2, CHUNK])
        s_t = sbuf("s_t", [P, N, 2 * P], F32R)
        f_q = sbuf("f_q", [D, N, 2 * P])
        w_hl = sbuf("w_hl", [P, N, 2 * D], F32R)
        k_raw = sbuf("k_raw", [D, D])
        k_hi = sbuf("k_hi", [D, D], F32R)
        k_lo = sbuf("k_lo", [D, D], F32R)
        q_sb = sbuf("q_sb", [D, D])
        o_sb = sbuf("o_sb", [P, OBUF, IR * D])
        w_raw = f_q[:, :, P:2 * P]

        kf_ps = psum("kf_ps", [D, 2, CHUNK])
        s_ps = psum("s_ps", [P, 2, CB // 2, PAIR])
        o_ps = psum("o_ps", [P, 2, IR, 2 * D])

        f_in = [sem(f"f_in{n}") for n in range(LOADS)]
        k_in, q_in = sem("k_in"), sem("q_in")
        w_in = [sem(f"w_in{n}") for n in range(WPIECES)]
        o_stored = [sem(f"o_stored{n}") for n in range(OBUF)]
        tail_stored = [sem(f"tail_stored{n}") for n in range(GROUP)]
        k_split = sem("k_split")
        fhi_done = sem("fhi_done")
        flo_done = sem("flo_done")
        kf_done = sem("kf_done")
        kf_copied = sem("kf_copied")
        s_done = sem("s_done")
        shi_done = sem("shi_done")
        slo_done = sem("slo_done")
        fq_done = sem("fq_done")
        whi_done = sem("whi_done")
        wlo_done = sem("wlo_done")
        o_done = sem("o_done")
        ohi_done = sem("ohi_done")
        out_done = sem("out_done")

        def arrived(eng, g, r):
            turn = (g - r) // GROUP if isinstance(g, int) else (g - r) >> 3
            eng.wait_ge(f_in[r // 2], turn * 16 + 16)

        def o_buffer(h, r):
            if isinstance(h, int) and h >= FRONT - STEPS:
                return f_ring[:, r, :].rearrange("p (i d) -> p i d", i=IR), tail_stored[r]
            return o_sb[:, r % OBUF, :].rearrange("p (i d) -> p i d", i=IR), o_stored[r % OBUF]

        def pieces(g):
            return [n for n in ([0, 1] if g == 0 else [g + 1]) if n < WPIECES]

        def wait(eng, semaphore, count):
            if not (isinstance(count, int) and count <= 0):
                eng.wait_ge(semaphore, count)

        def groups(eng, step):
            def one(j):
                base = j * GROUP
                col = (j % 4) * (GROUP * CB) if isinstance(j, int) else (j & 3) * (GROUP * CB)
                static = isinstance(j, int)
                for r in range(GROUP):
                    step(j, base, r, col, not static or j < GROUPS, not static or j >= LAG)
            for j in range(LAG + 1):
                one(j)
            with nc.Fori(LAG + 1, GROUPS - 1, engines=[eng.engine], hint_back_edge=True) as j:
                one(j)
            for j in range(GROUPS - 1, GROUPS + LAG):
                one(j)

        block = ctx.enter_context(nc.Block())

        @block.sync
        def _(sp):
            w_jid = w.rearrange("i j d -> j i d")

            def load_f(m, slot):
                sp.dma_start(f_ring[:, 2 * slot:2 * slot + 2, :],
                             f_t[bass.ds(m, 1), :, :, :].rearrange("o d c n -> (o d) c n")
                             ).then_inc(f_in[slot], 16)

            def load_w(n):
                rows = slice(n * WROWS, (n + 1) * WROWS)
                for half in range(2):
                    sp.dma_start(w_raw[half * N:(half + 1) * N, rows, :], w_jid[:, rows, :]
                                 ).then_inc(w_in[n], 16)

            def store(tile, i0, r, h):
                sp.wait_ge(out_done, h + 3)
                dst = out[bass.ds(tile * P, P), bass.ds(i0, IR), :]
                rows, stored = o_buffer(h, r)
                sp.dma_start(dst, rows).then_inc(stored, 16)

            load_f(0, 0)
            sp.dma_start(k_raw[:, :], k_t).then_inc(k_in, 16)
            for m in range(1, LOADS - 1):
                load_f(m, m)
            load_w(0)
            load_w(1)
            load_w(2)
            sp.dma_start(q_sb[:, :], q_t).then_inc(q_in, 16)

            def step(j, base, r, col, front, back):
                static = isinstance(j, int)
                if r % 2 == 0 and not (static and base + r + 6 >= FRONT):
                    wait(sp, s_done, base + r)
                    wait(sp, fq_done, base + r)
                    load_f(j * 4 + (r + 6) // 2, (r // 2 + 3) % LOADS)
                if static and base + r + 3 < WPIECES:
                    load_w(base + r + 3)
                if static:
                    h = base + r - STEPS - 1
                    if h >= 0:
                        store(h // STEPS, (h % STEPS) * IR, h % GROUP, h)
                elif r == 0:
                    store((j - LAG - 1) >> 1, ((j - LAG - 1) & 1) * (GROUP * IR) + (GROUP - 1) * IR,
                          GROUP - 1, base - STEPS - 1)
                else:
                    store((j - LAG) >> 1, ((j - LAG) & 1) * (GROUP * IR) + (r - 1) * IR,
                          r - 1, base + (r - 1 - STEPS))

            groups(sp, step)
            store(TILES - 1, (STEPS - 1) * IR, GROUP - 1, FRONT - 1)
            for n in range(OBUF):
                sp.wait_ge(o_stored[n], 16 * ((FRONT - STEPS) // OBUF))
            for n in range(GROUP):
                sp.wait_ge(tail_stored[n], 16 * (STEPS // GROUP))

        @block.scalar
        def _(act):
            def split_f(g, r):
                arrived(act, g, r)
                wait(act, kf_done, g)
                nc.scalar.activation(f_hi[:, :], f_ring[:, r, :], COPY).then_inc(fhi_done, 1)

            def copy_kf(g, r):
                act.wait_ge(kf_done, g + 1)
                wait(act, s_done, g - 1)
                nc.scalar.activation(kf[:, r % 2, :], kf_ps[:, r % 2, :], COPY).then_inc(kf_copied, 1)

            def store_s_hi(g, r, col):
                act.wait_ge(s_done, g + 1)
                for half in range(2):
                    rows = slice(half * N, (half + 1) * N)
                    ins = nc.scalar.activation(
                        s_t[rows, :, bass.ds(col + (r * CB + 4 * half), 4)],
                        s_ps[rows, r % 2, :, rows].rearrange("p k i -> p i k"), COPY)
                ins.then_inc(shi_done, 1)

            def copy_out_hi(h, r):
                act.wait_ge(o_done, h + 1)
                rows, stored = o_buffer(h, r)
                if stored in o_stored:
                    wait(act, stored, (h - r % OBUF) * (16 // OBUF))
                elif h < FRONT - STEPS + GROUP:
                    act.wait_ge(s_done, FRONT)
                    act.wait_ge(fq_done, FRONT)
                else:
                    act.wait_ge(stored, 16)
                nc.scalar.activation(rows, o_ps[:, r % 2, :, 0:D], COPY).then_inc(ohi_done, 1)

            act.wait_ge(k_in, 16)
            nc.scalar.activation(k_hi[:, :], k_raw[:, :], COPY).then_inc(k_split, 1)
            split_f(0, 0)
            copy_kf(0, 0)
            split_f(1, 1)

            def step(j, base, r, col, front, back):
                static = isinstance(j, int)
                g = base + r
                if back and not (static and g == STEPS):
                    copy_out_hi(base + (r - STEPS - 1), (r - 1) % GROUP)
                if front and not (static and g + 2 >= FRONT):
                    split_f(base + (r + 2), (r + 2) % GROUP)
                if front and not (static and g + 1 >= FRONT):
                    copy_kf(base + (r + 1), (r + 1) % GROUP)
                if front:
                    if r == 0:
                        wait(act, o_done, base - STEPS)
                    store_s_hi(g, r, col)
                for n in pieces(g) if static else []:
                    rows = slice(n * WROWS, (n + 1) * WROWS)
                    act.wait_ge(w_in[n], 32)
                    nc.scalar.activation(w_hl[:, rows, 0:D], w_raw[:, rows, :], COPY).then_inc(whi_done, 1)

            groups(act, step)
            copy_out_hi(FRONT - 1, GROUP - 1)

        @block.vector
        def _(dve):
            def split_f(g, r):
                dve.wait_ge(fhi_done, g + 1)
                wait(dve, kf_done, g)
                nc.vector.tensor_tensor(f_lo[:, :], f_ring[:, r, :], f_hi[:, :].bitcast(F32),
                                        ALU.subtract).then_inc(flo_done, 1)

            def store_s_lo(g, r, col):
                dve.wait_ge(shi_done, g + 1)
                for half in range(2):
                    rows = slice(half * N, (half + 1) * N)
                    other = slice((1 - half) * N, (2 - half) * N)
                    cols = bass.ds(col + (r * CB + 4 * half), 4)
                    ins = nc.vector.tensor_tensor(
                        s_t[other, :, cols],
                        s_ps[rows, r % 2, :, rows].rearrange("p k i -> p i k"),
                        s_t[rows, :, cols].bitcast(F32), ALU.subtract)
                ins.then_inc(slo_done, 1)

            def sum_out(h, r):
                dve.wait_ge(ohi_done, h + 1)
                rows, _ = o_buffer(h, r)
                nc.vector.tensor_tensor(rows, o_ps[:, r % 2, :, D:2 * D], rows,
                                        ALU.add).then_inc(out_done, 1)

            dve.sem_inc(out_done, 2)
            dve.wait_ge(k_split, 1)
            nc.vector.tensor_tensor(k_lo[:, :], k_raw[:, :], k_hi[:, :].bitcast(F32),
                                    ALU.subtract).then_inc(k_split, 1)
            split_f(0, 0)
            split_f(1, 1)

            def step(j, base, r, col, front, back):
                static = isinstance(j, int)
                g = base + r
                if back and not (static and g == STEPS):
                    sum_out(base + (r - STEPS - 1), (r - 1) % GROUP)
                if front and not (static and g + 2 >= FRONT):
                    split_f(base + (r + 2), (r + 2) % GROUP)
                if front:
                    store_s_lo(g, r, col)
                for n in pieces(g) if static else []:
                    rows = slice(n * WROWS, (n + 1) * WROWS)
                    dve.wait_ge(whi_done, n + 1)
                    nc.vector.tensor_tensor(w_hl[:, rows, D:2 * D], w_raw[:, rows, :],
                                            w_hl[:, rows, 0:D].bitcast(F32),
                                            ALU.subtract).then_inc(wlo_done, 1)

            groups(dve, step)
            sum_out(FRONT - 1, GROUP - 1)

        @block.gpsimd
        def _(pool):
            def copy_fq(g, r, col):
                arrived(pool, g, r)
                nc.gpsimd.tensor_copy(
                    f_q[:, :, bass.ds(col + r * CB, CB)].rearrange("d i (h k) -> d i h k", h=2),
                    f_ring[:, r, :].rearrange("d (k h i) -> d i h k", k=4, h=2)).then_inc(fq_done, 1)

            def step(j, base, r, col, front, back):
                static = isinstance(j, int)
                g = base + r
                if front:
                    if static and g == STEPS:
                        pool.wait_ge(wlo_done, WPIECES)
                    if r == 0:
                        wait(pool, o_done, base - STEPS)
                    copy_fq(g, r, col)

            groups(pool, step)

        @block.tensor
        def _(pe):
            def project(g, n):
                pe.wait_ge(flo_done, g + 1)
                wait(pe, kf_copied, g - 1)
                dst = kf_ps[:, n % 2, :]
                nc.tensor.matmul(dst, k_hi[:, :], f_hi[:, :], start=True, stop=False)
                nc.tensor.matmul(dst, k_hi[:, :], f_lo[:, :], start=False, stop=False)
                nc.tensor.matmul(dst, k_lo[:, :], f_hi[:, :], start=False, stop=True
                                 ).then_inc(kf_done, 1)

            def scores(g, n):
                pe.wait_ge(kf_copied, g + 1)
                wait(pe, slo_done, g - 1)
                for k in range(CB // 2):
                    cols = slice(k * PAIR, (k + 1) * PAIR)
                    ins = nc.tensor.matmul(s_ps[:, n % 2, k, :], kf[:, n % 2, cols],
                                           f_ring[:, n % GROUP, cols], start=True, stop=True)
                ins.then_inc(s_done, 1)

            def rows_out(tile_parity, n):
                for x in range(IR):
                    i = n * IR + x
                    cols = slice(tile_parity * P, (tile_parity + 1) * P)
                    nc.tensor.matmul(o_ps[:, n % 2, x, :], s_t[:, i, cols], w_hl[:, i, :],
                                     start=True, stop=False, skip_group_check=True)
                    ins = nc.tensor.matmul(o_ps[:, n % 2, x, 0:D], f_q[:, i, cols], q_sb[:, :],
                                           start=False, stop=True, skip_group_check=True)
                ins.then_inc(o_done, 1)

            def tile(base, parity, front=True, back=True, last=False):
                for n in range(STEPS):
                    if front and not (last and n == STEPS - 1):
                        project(base + (n + 1), n + 1)
                    if front:
                        scores(base + n, n)
                    if back:
                        if n == 0:
                            pe.wait_ge(slo_done, base)
                            pe.wait_ge(fq_done, base)
                        pe.wait_ge(out_done, base + (n - STEPS + 1))
                        rows_out(1 - parity, n)

            pe.wait_ge(k_split, 2)
            project(0, 0)
            tile(0, 0, back=False)
            pe.wait_ge(q_in, 16)
            pe.wait_ge(wlo_done, WPIECES)
            with nc.Fori(0, TILES // 2 - 1, engines=[pe.engine], hint_back_edge=True) as pair:
                base = pair * (2 * STEPS) + STEPS
                tile(base, 1)
                tile(base + STEPS, 0)
            tile(FRONT - STEPS, 1, last=True)
            tile(FRONT, 0, front=False)


def kernel(r_F, L0_rec_W, L0_rec_K_w, L0_rec_Q_w):
    import numpy as np
    import concourse.bacc as bacc
    from concourse.bass_utils import run_bass_kernel_spmd

    f = np.asarray(r_F).reshape(FRONT // 2, 2, 2, CB // 2, N, D)
    f_t = np.ascontiguousarray(f.transpose(0, 5, 1, 3, 2, 4)).reshape(FRONT // 2, D, 2, CHUNK)
    arrays = {
        "f_t": f_t,
        "k_t": np.ascontiguousarray(np.asarray(L0_rec_K_w).T),
        "q_t": np.ascontiguousarray(np.asarray(L0_rec_Q_w).T),
        "w": np.ascontiguousarray(np.asarray(L0_rec_W)),
    }
    nc = bacc.Bacc("TRN2", target_bir_lowering=False, num_devices=1, dynamic_dma_scratch_size=1024)
    args = [nc.dram_tensor(n, a.shape, F32, kind="ExternalInput").ap() for n, a in arrays.items()]
    out = nc.dram_tensor("out", (B, N, D), F32, kind="ExternalOutput").ap()
    build(nc, *args, out)
    r = run_bass_kernel_spmd(nc, [arrays], core_ids=[0])
    return r.results[0]["out"]
```
